# Optimizing a Trainium2 kernel written in Bass

```python
import numpy as np
import jax
import jax.numpy as jnp

def _softmax(x, axis=-1):
    return jax.nn.softmax(x, axis=axis)
def _gelu(x):
    return jax.nn.gelu(x, approximate=True)
def _silu(x):
    return jax.nn.silu(x)
def _sigmoid(x):
    return jax.nn.sigmoid(x)
def _layernorm(x, axis=-1, eps=1e-5):
    m = jnp.mean(x, axis=axis, keepdims=True)
    v = jnp.var(x, axis=axis, keepdims=True)
    return (x - m) / jnp.sqrt(v + eps)
def _scatter_add(tgt, idx, src, axis=0):
    return tgt.at[idx].add(src)
def _segment_sum(src, seg, n):
    return jax.ops.segment_sum(src, seg, n)

kernel_name = 'mk_conv_attn_hybrid_d2_conv_nhwc128_81caf2'

def setup_inputs(seed: int = 0):
    np.random.seed(seed)
    _w = jnp.asarray
    def _rec_inputs():
        import jax
        import jax.numpy as jnp
        _gk = jax.random.key(seed)
        x = -0.000929 + 1 * jax.random.normal(jax.random.fold_in(_gk, 1), (2, 64, 64, 128), jnp.float32)
        return x
    x = _rec_inputs()
    def _L0_conv_setup():
        import jax, jax.numpy as jnp
        import numpy as np
        import math
        D_MODEL = 128
        D_STATE = 16
        D_CONV = 3
        EXPAND = 2
        D_INNER = EXPAND * D_MODEL
        DT_RANK = math.ceil(D_MODEL / 16)
        B, H, W = (2, 64, 64)
        LN_EPS = 1e-05

        def _local_scan(x, Hh, Ww, w_h, w_w, flip=False, column_first=False):
            Bb, C = (x.shape[0], x.shape[1])
            Hg, Wg = (Hh // w_h, Ww // w_w)
            x = x.reshape(Bb, C, Hg, w_h, Wg, w_w)
            if column_first:
                x = x.transpose(0, 1, 4, 2, 5, 3)
            else:
                x = x.transpose(0, 1, 2, 4, 3, 5)
            x = x.reshape(Bb, C, -1)
            if flip:
                x = x[:, :, ::-1]
            return x

        def _selective_scan(u, delta, A, Bm, Cm, D, delta_bias):
            Bsz, Dch, L = u.shape
            K, N = (Bm.shape[1], A.shape[1])
            d = Dch // K
            delta = jax.nn.softplus(delta + delta_bias[None, :, None])
            A4 = A.reshape(K, d, N)
            u4 = u.reshape(Bsz, K, d, L)
            dt4 = delta.reshape(Bsz, K, d, L)

            def step(h, inp):
                ut, dt, bt, ct = inp
                dA = jnp.exp(dt[..., None] * A4)
                h = dA * h + (dt * ut)[..., None] * bt[:, :, None, :]
                y = jnp.einsum('bkdn,bkn->bkd', h, ct)
                return (h, y)
            xs_t = (u4.transpose(3, 0, 1, 2), dt4.transpose(3, 0, 1, 2), Bm.transpose(3, 0, 1, 2), Cm.transpose(3, 0, 1, 2))
            h0 = jnp.zeros((Bsz, K, d, N), u.dtype)
            _, ys = jax.lax.scan(step, h0, xs_t)
            y = ys.transpose(1, 2, 3, 0).reshape(Bsz, Dch, L)
            return y + u * D[None, :, None]
        key = jax.random.key(seed)
        ks = jax.random.split(key, 8)
        x = jax.random.normal(ks[0], (B, H, W, D_MODEL), jnp.float32)
        W_in = jax.random.normal(ks[1], (2 * D_INNER, D_MODEL), jnp.float32) * D_MODEL ** (-0.5)
        conv_w = jax.random.normal(ks[2], (D_INNER, 1, D_CONV, D_CONV), jnp.float32) * (1.0 / D_CONV)
        conv_b = jnp.zeros((D_INNER,), jnp.float32)
        x_proj_w = jax.random.normal(ks[3], (4, DT_RANK + 2 * D_STATE, D_INNER), jnp.float32) * D_INNER ** (-0.5)
        std = DT_RANK ** (-0.5)
        dt_proj_w = jax.random.uniform(ks[4], (4, D_INNER, DT_RANK), jnp.float32, -std, std)
        dt = jnp.exp(jax.random.uniform(ks[5], (4, D_INNER), jnp.float32) * (math.log(0.1) - math.log(0.001)) + math.log(0.001))
        dt = jnp.maximum(dt, 0.0001)
        dt_proj_b = dt + jnp.log(-jnp.expm1(-dt))
        A_logs = jnp.log(jnp.tile(jnp.arange(1, D_STATE + 1, dtype=jnp.float32)[None, :], (4 * D_INNER, 1)))
        Ds = jnp.ones((4 * D_INNER,), jnp.float32)
        ln_w = jnp.ones((D_INNER,), jnp.float32)
        ln_b = jnp.zeros((D_INNER,), jnp.float32)
        W_out = jax.random.normal(ks[6], (D_MODEL, D_INNER), jnp.float32) * D_INNER ** (-0.5)
        return dict(x=x, W_in=W_in, conv_w=conv_w, conv_b=conv_b, x_proj_w=x_proj_w, dt_proj_w=dt_proj_w, dt_proj_b=dt_proj_b, A_logs=A_logs, Ds=Ds, ln_w=ln_w, ln_b=ln_b, W_out=W_out)
    _L0_conv_all = _L0_conv_setup()
    _L0_conv_in = {k: v for k, v in _L0_conv_all.items() if k in ('W_in', 'conv_w', 'conv_b', 'x_proj_w', 'dt_proj_w', 'dt_proj_b', 'A_logs', 'Ds', 'ln_w', 'ln_b', 'W_out', )}
    del _L0_conv_all

    def _L1_attn_setup():
        import jax, jax.numpy as jnp
        import numpy as np
        B, T, D = (4, 2048, 128)
        key = jax.random.key(seed)
        k1, k2, k3 = jax.random.split(key, 3)
        x = jax.random.normal(k1, (B, T, D), dtype=jnp.float32)
        lim = 1.0 / np.sqrt(D)
        W = jax.random.uniform(k2, (3 * D, D), dtype=jnp.float32, minval=-lim, maxval=lim)
        b = jax.random.uniform(k3, (3 * D,), dtype=jnp.float32, minval=-lim, maxval=lim)
        return {'x': x, 'W': W, 'b': b}
    _L1_attn_all = _L1_attn_setup()
    _L1_attn_in = {k: v for k, v in _L1_attn_all.items() if k in ('W', 'b', )}
    del _L1_attn_all

    def _L1_ffn_setup():
        import jax, jax.numpy as jnp
        import numpy as np
        PADDED_SL = 8192
        TEMPERATURE = 1.0
        SIGMA_POW = 0.25

        def _stu_conv(phi, u, n):
            b, sl, d = u.shape
            sgn = jnp.where(jnp.arange(sl) % 2 == 0, 1.0, -1.0).astype(u.dtype)
            sgn3 = sgn[None, :, None]
            Vf = jnp.fft.rfft(phi, n=n, axis=0)
            Uf_p = jnp.fft.rfft(u, n=n, axis=1)
            Uf_m = jnp.fft.rfft(u * sgn3, n=n, axis=1)
            U_plus = jnp.fft.irfft(Vf[None, :, :, None] * Uf_p[:, :, None, :], n=n, axis=1)[:, :sl]
            U_minus = jnp.fft.irfft(Vf[None, :, :, None] * Uf_m[:, :, None, :], n=n, axis=1)[:, :sl]
            U_minus = U_minus * sgn[None, :, None, None]
            return (U_plus, U_minus)

        def _compute_spectral(u, sigma, phi, Mpp, Mpm):
            U_plus, U_minus = _stu_conv(phi, u, PADDED_SL)
            s = sigma ** SIGMA_POW
            out = jnp.einsum('btkd,k,kde->bte', U_plus, s, Mpp)
            out = out + jnp.einsum('btkd,k,kde->bte', U_minus, s, Mpm)
            return out

        def _compute_ar_u(Mu, u):
            sl = u.shape[1]
            out = jnp.zeros(u.shape[:2] + (Mu.shape[-1],), dtype=u.dtype)
            for i in range(Mu.shape[0]):
                ui = jnp.pad(u, ((0, 0), (i, 0), (0, 0)))[:, :sl]
                out = out + jnp.einsum('btd,de->bte', ui, Mu[i])
            return out

        def _stu(u, sigma, phi, Mu, Mpp, Mpm):
            return _compute_spectral(u, sigma, phi, Mpp, Mpm) + _compute_ar_u(Mu, u)
        key = jax.random.key(seed)
        ks = jax.random.split(key, 8)
        b, sl, d, K, k_u = (2, 4096, 128, 16, 3)
        x = jax.random.normal(ks[0], (b, sl, d), dtype=jnp.float32)
        sigma = jax.random.uniform(ks[1], (K,), dtype=jnp.float32, minval=0.001, maxval=1.0)
        phi = jax.random.normal(ks[2], (sl, K), dtype=jnp.float32) / np.sqrt(sl)
        M_u = jax.random.normal(ks[3], (4, k_u, d, d), dtype=jnp.float32) * 0.02
        M_phi_plus = jax.random.normal(ks[4], (4, K, d, d), dtype=jnp.float32) * 0.02
        M_phi_minus = jax.random.normal(ks[5], (4, K, d, d), dtype=jnp.float32) * 0.02
        log_weights = jnp.ones((4,), dtype=jnp.float32)
        u01 = jax.random.uniform(ks[6], (4,), dtype=jnp.float32, minval=1e-06, maxval=1.0 - 1e-06)
        gumbel = -jnp.log(-jnp.log(u01))
        return {'x': x, 'sigma': sigma, 'phi': phi, 'M_u': M_u, 'M_phi_plus': M_phi_plus, 'M_phi_minus': M_phi_minus, 'log_weights': log_weights, 'gumbel': gumbel}
    _L1_ffn_all = _L1_ffn_setup()
    _L1_ffn_in = {k: v for k, v in _L1_ffn_all.items() if k in ('sigma', 'phi', 'M_u', 'M_phi_plus', 'M_phi_minus', 'log_weights', 'gumbel', )}
    del _L1_ffn_all

    return {
        "x": x,
        "L0_conv_W_in": _L0_conv_in["W_in"],
        "L0_conv_conv_w": _L0_conv_in["conv_w"],
        "L0_conv_conv_b": _L0_conv_in["conv_b"],
        "L0_conv_x_proj_w": _L0_conv_in["x_proj_w"],
        "L0_conv_dt_proj_w": _L0_conv_in["dt_proj_w"],
        "L0_conv_dt_proj_b": _L0_conv_in["dt_proj_b"],
        "L0_conv_A_logs": _L0_conv_in["A_logs"],
        "L0_conv_Ds": _L0_conv_in["Ds"],
        "L0_conv_ln_w": _L0_conv_in["ln_w"],
        "L0_conv_ln_b": _L0_conv_in["ln_b"],
        "L0_conv_W_out": _L0_conv_in["W_out"],
        "L1_attn_W": _L1_attn_in["W"],
        "L1_attn_b": _L1_attn_in["b"],
        "L1_ffn_sigma": _L1_ffn_in["sigma"],
        "L1_ffn_phi": _L1_ffn_in["phi"],
        "L1_ffn_M_u": _L1_ffn_in["M_u"],
        "L1_ffn_M_phi_plus": _L1_ffn_in["M_phi_plus"],
        "L1_ffn_M_phi_minus": _L1_ffn_in["M_phi_minus"],
        "L1_ffn_log_weights": _L1_ffn_in["log_weights"],
        "L1_ffn_gumbel": _L1_ffn_in["gumbel"],
    }

def reference(x, L0_conv_W_in, L0_conv_conv_w, L0_conv_conv_b, L0_conv_x_proj_w, L0_conv_dt_proj_w, L0_conv_dt_proj_b, L0_conv_A_logs, L0_conv_Ds, L0_conv_ln_w, L0_conv_ln_b, L0_conv_W_out, L1_attn_W, L1_attn_b, L1_ffn_sigma, L1_ffn_phi, L1_ffn_M_u, L1_ffn_M_phi_plus, L1_ffn_M_phi_minus, L1_ffn_log_weights, L1_ffn_gumbel):
    import jax
    import jax.numpy as jnp
    def _L0_conv_ref(x, W_in, conv_w, conv_b, x_proj_w, dt_proj_w, dt_proj_b, A_logs, Ds, ln_w, ln_b, W_out):
        import jax, jax.numpy as jnp
        import numpy as np
        import math
        D_MODEL = 128
        D_STATE = 16
        D_CONV = 3
        EXPAND = 2
        D_INNER = EXPAND * D_MODEL
        DT_RANK = math.ceil(D_MODEL / 16)
        B, H, W = (2, 64, 64)
        LN_EPS = 1e-05

        def _local_scan(x, Hh, Ww, w_h, w_w, flip=False, column_first=False):
            Bb, C = (x.shape[0], x.shape[1])
            Hg, Wg = (Hh // w_h, Ww // w_w)
            x = x.reshape(Bb, C, Hg, w_h, Wg, w_w)
            if column_first:
                x = x.transpose(0, 1, 4, 2, 5, 3)
            else:
                x = x.transpose(0, 1, 2, 4, 3, 5)
            x = x.reshape(Bb, C, -1)
            if flip:
                x = x[:, :, ::-1]
            return x

        def _selective_scan(u, delta, A, Bm, Cm, D, delta_bias):
            Bsz, Dch, L = u.shape
            K, N = (Bm.shape[1], A.shape[1])
            d = Dch // K
            delta = jax.nn.softplus(delta + delta_bias[None, :, None])
            A4 = A.reshape(K, d, N)
            u4 = u.reshape(Bsz, K, d, L)
            dt4 = delta.reshape(Bsz, K, d, L)

            def step(h, inp):
                ut, dt, bt, ct = inp
                dA = jnp.exp(dt[..., None] * A4)
                h = dA * h + (dt * ut)[..., None] * bt[:, :, None, :]
                y = jnp.einsum('bkdn,bkn->bkd', h, ct)
                return (h, y)
            xs_t = (u4.transpose(3, 0, 1, 2), dt4.transpose(3, 0, 1, 2), Bm.transpose(3, 0, 1, 2), Cm.transpose(3, 0, 1, 2))
            h0 = jnp.zeros((Bsz, K, d, N), u.dtype)
            _, ys = jax.lax.scan(step, h0, xs_t)
            y = ys.transpose(1, 2, 3, 0).reshape(Bsz, Dch, L)
            return y + u * D[None, :, None]
        Bb, Hh, Ww, _ = x.shape
        L = Hh * Ww
        d_inner = conv_b.shape[0]
        dt_rank = dt_proj_w.shape[2]
        N = A_logs.shape[1]
        xz = x @ W_in.T
        xc, z = jnp.split(xz, 2, axis=-1)
        xc = xc.transpose(0, 3, 1, 2)
        xc = jax.lax.conv_general_dilated(xc, conv_w, (1, 1), ((1, 1), (1, 1)), dimension_numbers=('NCHW', 'OIHW', 'NCHW'), feature_group_count=d_inner) + conv_b[None, :, None, None]
        xc = jax.nn.silu(xc)
        w_h, w_w = (Hh // 4, Ww // 4)
        x1 = _local_scan(xc, Hh, Ww, w_h, w_w)
        x2 = _local_scan(xc, Hh, Ww, w_h, w_w, column_first=True)
        x3 = _local_scan(xc, Hh, Ww, w_h, w_w, flip=True)
        x4 = _local_scan(xc, Hh, Ww, w_h, w_w, column_first=True, flip=True)
        xs = jnp.stack([x1, x2, x3, x4], axis=1)
        x_dbl = jnp.einsum('bkdl,kcd->bkcl', xs, x_proj_w)
        dts, Bs, Cs = jnp.split(x_dbl, [dt_rank, dt_rank + N], axis=2)
        dts = jnp.einsum('bkrl,kdr->bkdl', dts, dt_proj_w)
        u = xs.reshape(Bb, -1, L)
        delta = dts.reshape(Bb, -1, L)
        As = -jnp.exp(A_logs)
        out_y = _selective_scan(u, delta, As, Bs, Cs, Ds, dt_proj_b.reshape(-1)).reshape(Bb, 4, -1, L)
        inv_y = out_y[:, 2:4, :, ::-1]
        wh_y = out_y[:, 1].reshape(Bb, -1, Ww, Hh).transpose(0, 1, 3, 2).reshape(Bb, -1, L)
        invwh_y = inv_y[:, 1].reshape(Bb, -1, Ww, Hh).transpose(0, 1, 3, 2).reshape(Bb, -1, L)
        y = out_y[:, 0] + inv_y[:, 0] + wh_y + invwh_y
        y = y.transpose(0, 2, 1).reshape(Bb, Hh, Ww, -1)
        mu = jnp.mean(y, axis=-1, keepdims=True)
        var = jnp.mean(jnp.square(y - mu), axis=-1, keepdims=True)
        y = (y - mu) * jax.lax.rsqrt(var + LN_EPS) * ln_w + ln_b
        y = y * jax.nn.silu(z)
        return y @ W_out.T

    def _L1_attn_ref(x, W, b):
        import jax, jax.numpy as jnp
        import numpy as np
        B, T, D = (4, 2048, 128)
        Bx, Tx, Dx = x.shape
        qkv = (x @ W.T + b).reshape(Bx, Tx, 3, Dx)
        q, k, v = (qkv[:, :, 0], qkv[:, :, 1], qkv[:, :, 2])
        q = jax.nn.elu(q) + 1.0
        k = jax.nn.elu(k) + 1.0
        kv = jnp.einsum('bti,btj->btij', k, v)
        kv_cum = jnp.cumsum(kv, axis=1)
        k_cum = jnp.cumsum(k, axis=1)
        num = jnp.einsum('bti,btij->btj', q, kv_cum)
        den = jnp.einsum('bti,bti->bt', q, k_cum)[..., None] + 1e-06
        return num / den

    def _L1_ffn_ref(x, sigma, phi, M_u, M_phi_plus, M_phi_minus, log_weights, gumbel):
        import jax, jax.numpy as jnp
        import numpy as np
        PADDED_SL = 8192
        TEMPERATURE = 1.0
        SIGMA_POW = 0.25

        def _stu_conv(phi, u, n):
            b, sl, d = u.shape
            sgn = jnp.where(jnp.arange(sl) % 2 == 0, 1.0, -1.0).astype(u.dtype)
            sgn3 = sgn[None, :, None]
            Vf = jnp.fft.rfft(phi, n=n, axis=0)
            Uf_p = jnp.fft.rfft(u, n=n, axis=1)
            Uf_m = jnp.fft.rfft(u * sgn3, n=n, axis=1)
            U_plus = jnp.fft.irfft(Vf[None, :, :, None] * Uf_p[:, :, None, :], n=n, axis=1)[:, :sl]
            U_minus = jnp.fft.irfft(Vf[None, :, :, None] * Uf_m[:, :, None, :], n=n, axis=1)[:, :sl]
            U_minus = U_minus * sgn[None, :, None, None]
            return (U_plus, U_minus)

        def _compute_spectral(u, sigma, phi, Mpp, Mpm):
            U_plus, U_minus = _stu_conv(phi, u, PADDED_SL)
            s = sigma ** SIGMA_POW
            out = jnp.einsum('btkd,k,kde->bte', U_plus, s, Mpp)
            out = out + jnp.einsum('btkd,k,kde->bte', U_minus, s, Mpm)
            return out

        def _compute_ar_u(Mu, u):
            sl = u.shape[1]
            out = jnp.zeros(u.shape[:2] + (Mu.shape[-1],), dtype=u.dtype)
            for i in range(Mu.shape[0]):
                ui = jnp.pad(u, ((0, 0), (i, 0), (0, 0)))[:, :sl]
                out = out + jnp.einsum('btd,de->bte', ui, Mu[i])
            return out

        def _stu(u, sigma, phi, Mu, Mpp, Mpm):
            return _compute_spectral(u, sigma, phi, Mpp, Mpm) + _compute_ar_u(Mu, u)
        T = x.shape[1]
        outs = []
        for i, frac in enumerate((1, 2, 4, 8)):
            xi = x[:, :T // frac]
            si = _stu(xi, sigma, phi, M_u[i], M_phi_plus[i], M_phi_minus[i])
            si = jnp.pad(si, ((0, 0), (0, T - si.shape[1]), (0, 0)))
            outs.append(si)
        y_soft = jax.nn.softmax((log_weights + gumbel) / TEMPERATURE)
        y_hard = jax.nn.one_hot(jnp.argmax(y_soft), 4, dtype=y_soft.dtype)
        weights = y_hard - jax.lax.stop_gradient(y_soft) + y_soft
        stacked = jnp.stack(outs, axis=-1)
        return jnp.sum(stacked * weights, axis=-1)

    def _gn(v, G=32, eps=1e-5):
        B_, H_, W_, C_ = v.shape
        g = v.reshape(B_, H_, W_, G, C_ // G)
        m = jnp.mean(g, axis=(1, 2, 4), keepdims=True)
        s = jnp.var(g, axis=(1, 2, 4), keepdims=True)
        return ((g - m) / jnp.sqrt(s + eps)).reshape(v.shape)

    def _ln_c(v, eps=1e-6):
        m = jnp.mean(v, axis=-1, keepdims=True)
        s = jnp.var(v, axis=-1, keepdims=True)
        return (v - m) / jnp.sqrt(s + eps)

    def _ln_t(v, eps=1e-5):
        m = jnp.mean(v, axis=-1, keepdims=True)
        s = jnp.var(v, axis=-1, keepdims=True)
        return (v - m) / jnp.sqrt(s + eps)

    def _to_tokens(v):
        B_, H_, W_, C_ = v.shape
        return v.reshape(B_, H_ * W_, C_)
    def _from_tokens(t, like):
        return t.reshape(like.shape)

    x = x + _L0_conv_ref(_gn(x), L0_conv_W_in, L0_conv_conv_w, L0_conv_conv_b, L0_conv_x_proj_w, L0_conv_dt_proj_w, L0_conv_dt_proj_b, L0_conv_A_logs, L0_conv_Ds, L0_conv_ln_w, L0_conv_ln_b, L0_conv_W_out)
    t = _to_tokens(x)
    t = t + _L1_attn_ref(_ln_t(t), L1_attn_W, L1_attn_b)
    t = t + _L1_ffn_ref(_ln_t(t), L1_ffn_sigma, L1_ffn_phi, L1_ffn_M_u, L1_ffn_M_phi_plus, L1_ffn_M_phi_minus, L1_ffn_log_weights, L1_ffn_gumbel)
    x = _from_tokens(t, x)
    return x


_drawn_inputs = setup_inputs


def setup_inputs(seed=0):
    import zlib

    import numpy as np

    out = dict(_drawn_inputs(seed))
    spreads = {'L0_conv_conv_b': (0.0, 0.1),
     'L0_conv_Ds': (1.0, 0.2),
     'L0_conv_ln_w': (1.0, 0.2),
     'L0_conv_ln_b': (0.0, 0.1),
     'L1_ffn_log_weights': (1.0, 0.2)}
    factors = {'L0_conv_dt_proj_w': 4.39}
    for name, (base, spread) in spreads.items():
        noise = np.random.default_rng([zlib.crc32(name.encode()), seed]).standard_normal(out[name].shape)
        drawn = base * np.exp(spread * noise) if base else spread * noise
        out[name] = jnp.asarray(drawn.astype(out[name].dtype))
    for name, factor in factors.items():
        out[name] = (out[name] * factor).astype(out[name].dtype)
    return out
```

```python
from contextlib import ExitStack

import concourse.bass as bass
import numpy as np
from concourse import mybir

fp32 = mybir.dt.float32
bf16 = mybir.dt.bfloat16
fp32r = mybir.dt.float32r
ALU = mybir.AluOpType
ACT = mybir.ActivationFunctionType
ds = bass.ds

P = 128
NB, H, W, C = 2, 64, 64, 128
T = H * W
DI = 256
DT2 = DI // P
NK, NS, NR = 4, 16, 8
WIN = 16
L = 512
NCH = T // L
START = 16
B_ROW, C_ROW = 32, 80


def scan_order(view, order, group, half):
    if order == 0:
        v = view[:, ds(group * 1024, 1024)].rearrange("p (w i j) -> p i w j", w=4, i=WIN)
        return v[:, half * 8:half * 8 + 8]
    v = view.rearrange("p (w x) -> p w x", w=4)[:, :, ds(group * 256, 256)]
    v = v.rearrange("p w (j i) -> p i w j", j=WIN)
    return v[:, half * 8:half * 8 + 8]


def start_counts(nc, semaphores):
    with nc.Block() as block:
        @block.sync
        def _(sp):
            for x in semaphores:
                for one in x if isinstance(x, list) else [x]:
                    sp.sem_inc(one, START)


def constants(nc, m, io):
    with ExitStack() as ctx:
        sb = lambda n, s, d=fp32: ctx.enter_context(nc.sbuf_tensor(n, s, d))
        sem = lambda n: ctx.enter_context(nc.semaphore(n))
        w_in = sb("w_in", [P, 4, C])
        cw = sb("cw", [P, DT2, 9])
        xp = sb("xp", [40, NK, DI])
        dtp = sb("dtp", [P, NK * DT2, NR])
        w_out = sb("w_out", [P, DI])
        w_qkv = sb("w_qkv", [P, 3, C])
        diag = sb("diag", [P, 2, 9, P])
        ps = [ctx.enter_context(nc.psum_tensor(f"wps{i}", [P, 512], fp32)) for i in range(8)]
        loaded, made, idmade = sem("w_loaded"), sem("w_const"), sem("w_ident")
        neg_a, diagged, multiplied, copied = sem("w_nega"), sem("w_diag"), sem("w_mm"), sem("w_copied")
        zeroed = sem("w_zeroed")
        block = ctx.enter_context(nc.Block())
        loads = [
            (w_in[:, :, :], io["W_in"].rearrange("(t p) c -> p t c", p=P)),
            (cw[:, :, :], io["conv_w"].rearrange("(t p) a i j -> p t (a i j)", p=P)),
            (xp[:, :, :], io["x_proj_w"].rearrange("k r d -> r k d")),
            (dtp[:, :, :], io["dt_proj_w"].rearrange("k (t p) r -> p (k t) r", p=P)),
            (w_out[:, :], io["W_out"]),
            (w_qkv[:, :, :], io["attn_W"].rearrange("(t p) c -> p t c", p=P)),
            (m.conv_b[:, :], io["conv_b"].rearrange("(t p) -> p t", p=P)),
            (m.dt_b[:, :], io["dt_proj_b"].rearrange("k (t p) -> p (k t)", p=P)),
            (m.a_neg[:, :, :], io["A_logs"].rearrange("(k p) n -> p k n", p=P)),
            (m.d_skip[:, 0:8], io["Ds"].rearrange("(k p) -> p k", p=P)),
            (m.ln_w[:, :], io["ln_w"].rearrange("(t p) -> p t", p=P)),
            (m.ln_b[:, :], io["ln_b"].rearrange("(t p) -> p t", p=P)),
            (m.b_qkv[:, :], io["attn_b"].rearrange("(t p) -> p t", p=P)),
            (m.b_v[:, :], io["attn_b"][256:384].partition_broadcast(P)),
        ]

        @block.sync
        def _(sp):
            with nc.allow_non_contiguous_dma(reason="small vectors, one value a channel"):
                for dst, src in loads:
                    sp.dma_start(dst, src).then_inc(loaded, 16)

        @block.gpsimd
        def _(pool):
            pool.memset(m.ident[:, :], 0.0).then_inc(idmade, 1)
            pool.memset(m.group[:, :], 0.25).then_inc(idmade, 1)
            pool.memset(m.select[:, :, :], 0.0).then_inc(idmade, 1)
            pool.memset(m.mean256[:, :], 1.0 / DI).then_inc(made, 1)
            pool.wait_ge(idmade, 3)
            pool.affine_select(out=m.ident[:, :], in_=m.ident[:, :], compare_op=ALU.not_equal, fill=1.0,
                               base=0, pattern=[[-1, P]], channel_multiplier=1).then_inc(made, 1)
            g = m.group[:, :].rearrange("p (g c) -> p g c", c=4)
            pool.affine_select(out=g, in_=g, compare_op=ALU.is_ge, fill=0.0, base=0,
                               pattern=[[-4, 32], [0, 4]], channel_multiplier=1).then_inc(idmade, 1)
            pool.wait_ge(idmade, 4)
            pool.affine_select(out=g, in_=g, compare_op=ALU.is_ge, fill=0.0, base=3,
                               pattern=[[4, 32], [0, 4]], channel_multiplier=-1).then_inc(made, 1)
            for part in range(6):
                row = B_ROW + NS * part
                s = m.select[:, NS * (part // 3):NS * (part // 3) + NS, :]
                pool.affine_select(out=s, in_=s, compare_op=ALU.not_equal, fill=1.0, base=-row,
                                   pattern=[[-1, NS], [0, P]], channel_multiplier=1).then_inc(idmade, 1)
                pool.wait_ge(idmade, 5 + part)
            pool.memset(m.minus[:, :], 0.0).then_inc(idmade, 1)
            pool.wait_ge(idmade, 11)
            v = 11
            for column, parts in ((0, (1, 2, 4, 5)), (1, (2, 5))):
                for part in parts:
                    row = B_ROW + NS * part
                    s = m.minus[:, column, :]
                    pool.affine_select(out=s, in_=s, compare_op=ALU.not_equal, fill=-1.0, base=-row,
                                       pattern=[[-1, NS]], channel_multiplier=1).then_inc(idmade, 1)
                    v += 1
                    pool.wait_ge(idmade, v)
            pool.memset(m.causal[:, :], 1.0).then_inc(idmade, 1)
            pool.wait_ge(idmade, v + 1)
            pool.affine_select(out=m.causal[:, :], in_=m.causal[:, :], compare_op=ALU.is_ge, fill=0.0,
                               base=0, pattern=[[1, P]], channel_multiplier=-1).then_inc(made, 1)

        @block.scalar
        def _(act):
            act.wait_ge(loaded, 16 * len(loads))
            act.activation(m.a_neg[:, :, :], m.a_neg[:, :, :], ACT.Exp).then_inc(neg_a, 1)

        @block.vector
        def _(dve):
            dve.memset(m.eps[:, 0:1], 1e-5).then_inc(zeroed, 1)
            dve.memset(m.xproj[:, :, :], 0.0).then_inc(zeroed, 1)
            dve.wait_ge(made, 4)
            dve.tensor_reduce(m.part_mask[:, :], m.minus[:, :, :], axis=mybir.AxisListType.X,
                              op=ALU.add).then_inc(zeroed, 1)
            dve.wait_ge(loaded, 16 * len(loads))
            dve.wait_ge(neg_a, 1)
            dve.tensor_scalar(m.a_neg[:, :, :], m.a_neg[:, :, :], -1.0, None, ALU.mult).then_inc(zeroed, 1)
            dve.tensor_tensor(m.d_skip[:, 8:10], m.d_skip[:, 0:2], m.d_skip[:, 4:6], ALU.add).then_inc(zeroed, 1)
            dve.tensor_tensor(m.d_skip[:, 10:12], m.d_skip[:, 2:4], m.d_skip[:, 6:8], ALU.add).then_inc(zeroed, 1)
            for t in range(DT2):
                if t:
                    dve.wait_ge(multiplied, t)
                for tap in range(9):
                    dve.tensor_scalar(diag[:, t, tap, :], m.ident[:, :], cw[:, t, tap:tap + 1], None,
                                      ALU.mult).then_inc(diagged, 1)
            dve.wait_ge(zeroed, 6)
            done = 0

            def out_of(dst, src, after):
                nonlocal done
                dve.wait_ge(multiplied, after)
                dve.tensor_copy(dst, src).then_inc(copied, 1)
                done += 1

            for t in range(DT2):
                for part in range(3):
                    n = min(4, 9 - 4 * part)
                    out_of(m.w_conv[:, t, 4 * part:4 * part + n, :],
                           ps[3 * t + part][:, 0:n * P].rearrange("p (a b) -> p a b", b=P), 1 + t)
            out_of(m.w_z[:, :, :], ps[6][:, 0:256].rearrange("p (a b) -> p a b", b=P), 3)
            out_of(m.w_o[:, :, :], ps[6][:, 256:512].rearrange("p (a b) -> p a b", b=P), 3)
            out_of(m.w_attn[:, :, :], ps[7][:, 0:384].rearrange("p (a b) -> p a b", b=P), 4)
            for i in range(NK * DT2):
                src = ps[i // 4][:, (i % 4) * 40:(i % 4) * 40 + 40]
                out_of(m.xproj[:, i, 0:NR], src[:, 0:NR], 5)
                for kind, row in ((0, B_ROW), (1, C_ROW)):
                    out_of(m.xproj[:, i, row:row + 48].rearrange("p (r n) -> p r n", r=3),
                           src[:, NR + NS * kind:NR + NS * kind + NS].unsqueeze(1).broadcast_to([P, 3, NS]), 5)
            for i in range(2):
                out_of(m.w_dt[0:NR, 4 * i:4 * i + 4, :], ps[2 + i][0:NR, :].rearrange("p (a b) -> p a b", b=P), 6)

        @block.tensor
        def _(pe):
            pe.wait_ge(loaded, 16 * len(loads))
            pe.wait_ge(made, 4)
            for t in range(DT2):
                pe.wait_ge(diagged, 9 * (t + 1))
                for tap in range(9):
                    last = pe.matmul(ps[3 * t + tap // 4][:, (tap % 4) * P:(tap % 4) * P + P], w_in[:, t, :],
                                     diag[:, t, tap, :], start=True, stop=True)
                last.then_inc(multiplied, 1)
            for t in range(DT2):
                pe.transpose(ps[6][:, t * P:t * P + P], w_in[:, 2 + t, :], m.ident[:, :])
                last = pe.transpose(ps[6][:, 256 + t * P:256 + t * P + P], w_out[:, t * P:t * P + P], m.ident[:, :])
            last.then_inc(multiplied, 1)
            for t in range(3):
                last = pe.transpose(ps[7][:, t * P:t * P + P], w_qkv[:, t, :], m.ident[:, :])
            last.then_inc(multiplied, 1)
            pe.wait_ge(copied, 6)
            for k in range(NK):
                for t in range(DT2):
                    i = DT2 * k + t
                    last = pe.transpose(ps[i // 4][:, (i % 4) * 40:(i % 4) * 40 + 40],
                                        xp[:, k, t * P:t * P + P], m.ident[0:40, 0:40])
            last.then_inc(multiplied, 1)
            for i in range(NK * DT2):
                last = pe.transpose(ps[2 + i // 4][0:NR, (i % 4) * P:(i % 4) * P + P], dtp[:, i, :], m.ident[:, :])
            last.then_inc(multiplied, 1)


def convolution(nc, m, io, b):
    with ExitStack() as ctx:
        sb = lambda n, s, d=fp32: ctx.enter_context(nc.sbuf_tensor(n, s, d))
        x_tok = sb("x_tok", [P, T // P, C])
        x_ch = sb("x_ch", [P, T])
        padded = sb("padded", [P, H + 2, W + 2])
        stats = sb("gn_stats", [P, NCH, 6])
        mv = sb("gn_mv", [P, 2])
        dev = sb("gn_dev", [P, 6])
        gate = sb("gate_out", [P, 2, DT2, L])
        s = m.sem_a
        pt = [ctx.enter_context(nc.psum_tensor(f"pt{i}", [P, L], fp32)) for i in range(2)]
        pg = ctx.enter_context(nc.psum_tensor("pg", [P, L], fp32))
        pc = [ctx.enter_context(nc.psum_tensor(f"pc{i}", [P, L], fp32)) for i in range(2)]
        pz = [ctx.enter_context(nc.psum_tensor(f"pz{i}", [P, L], fp32)) for i in range(2)]
        block = ctx.enter_context(nc.Block())
        NG = H // WIN

        @block.sync
        def _(sp):
            x_b = io["x"][ds(b, 1), :, :].rearrange("b (t p) c -> p (b t) c", p=P)
            for i in range(4):
                sp.dma_start(x_tok[:, 8 * i:8 * i + 8, :], x_b[:, 8 * i:8 * i + 8, :]).then_inc(s["x_in"][i], 16)
            with sp.Fori(0, NG) as g:
                for half in range(2):
                    sp.wait_ge(s["gated"], START + b * 17 + g * 4 + (2 * half + 3))
                    sp.dma_start(m.gate_dram[ds(b, 1), :, :, ds(g * 1024 + half * L, L)].rearrange("b p t l -> (b p) t l"),
                                 gate[:, half, :, :]).then_inc(s["gate_out"][half], 16)

        @block.gpsimd
        def _(pool):
            for half in range(2):
                pool.wait_ge(s["gate_out"][half], START + b * 64 + 64)

        @block.tensor
        def _(pe):
            for c in range(NCH):
                if c % 2 == 0:
                    pe.wait_ge(s["x_in"][c // 2], START + b * 16 + 16)
                if c >= 2:
                    pe.wait_ge(s["x_ch"], START + b * NCH + (c - 1))
                for i in range(4):
                    last = pe.transpose(pt[c % 2][:, i * P:i * P + P], x_tok[:, 4 * c + i, :], m.ident[:, :])
                last.then_inc(s["x_t"], 1)
            pe.wait_ge(s["gn"], START + b * 5 + 1)
            pe.matmul(pg[:, 0:1], m.group[:, :], mv[:, 0:1], start=True, stop=True).then_inc(s["gn_mm"], 1)
            pe.wait_ge(s["gn"], START + b * 5 + 3)
            pe.matmul(pg[:, 0:1], m.group[:, :], dev[:, 1:2], start=True, stop=True).then_inc(s["gn_mm"], 1)
            with pe.Fori(0, NG) as g:
                pe.wait_ge(s["normed"], START + b + 1)
                for half in range(2):
                    for t in range(DT2):
                        pe.wait_ge(s["gated"], START + b * 17 + g * 4 + (2 * half + t))
                        for tap in range(9):
                            di, dj = divmod(tap, 3)
                            last = pe.matmul(pc[t][:, :].rearrange("p (i j) -> p i j", j=W), m.w_conv[:, t, tap, :],
                                             padded[:, ds(g * WIN + (8 * half + di), 8), dj:dj + W],
                                             start=tap == 0, stop=tap == 8)
                        last.then_inc(s["conv_mm"], 1)
                        pe.matmul(pz[t][:, :].rearrange("p (i j) -> p i j", j=W), m.w_z[:, t, :],
                                  padded[:, ds(g * WIN + (8 * half + 1), 8), 1:1 + W],
                                  start=True, stop=True).then_inc(s["gate_mm"], 1)

        @block.scalar
        def _(act):
            for c in range(NCH):
                act.wait_ge(s["x_t"], START + b * NCH + (c + 1))
                act.copy(x_ch[:, c * L:c * L + L], pt[c % 2][:, :]).then_inc(s["x_ch"], 1)
            act.wait_ge(s["gn"], START + b * 5 + 4)
            act.activation(dev[:, 3:4], dev[:, 2:3], ACT.Sqrt, bias=m.eps[:, 0:1]).then_inc(s["gn_sqrt"], 1)
            act.sem_inc(s["gated"], 1)
            with act.Fori(0, NG) as g:
                for half in range(2):
                    for t in range(DT2):
                        act.wait_ge(s["conv_mm"], START + b * 16 + g * 4 + (2 * half + t + 1))
                        src = pc[t][:, :].rearrange("p (i w j) -> p i w j", i=8, w=4)
                        act.activation(scan_order(m.s1[:, t, :], 0, g, half), src, ACT.Silu,
                                       bias=m.conv_b[:, t:t + 1])
                        act.activation(scan_order(m.s2[:, t, :], 1, g, half), src, ACT.Silu,
                                       bias=m.conv_b[:, t:t + 1])
                        act.wait_ge(s["gate_mm"], START + b * 16 + g * 4 + (2 * half + t + 1))
                        act.wait_ge(s["gate_out"][half], START + b * 64 + g * 16)
                        act.activation(gate[:, half, t, :], pz[t][:, :], ACT.Silu).then_inc(s["gated"], 1)

        @block.vector
        def _(dve):
            dve.memset(padded[:, :, :], 0.0).then_inc(s["padded"], 1)
            for c in range(NCH):
                dve.wait_ge(s["x_ch"], START + b * NCH + (c + 1))
                dve.bn_stats(stats[:, c, :], x_ch[:, c * L:c * L + L]).then_inc(s["stats"], 1)
            dve.wait_ge(s["stats"], START + b * NCH + NCH)
            dve.memset(m.idle[:, :], 0.0)
            dve.bn_aggr(mv[:, :], stats[:, :, :]).then_inc(s["gn"], 1)
            dve.wait_ge(s["gn_mm"], START + b * 2 + 1)
            dve.tensor_scalar(dev[:, 0:1], mv[:, 0:1], pg[:, 0:1], None, ALU.subtract)
            dve.tensor_copy(dev[:, 5:6], pg[:, 0:1]).then_inc(s["gn"], 1)
            dve.wait_ge(s["gn"], START + b * 5 + 2)
            dve.scalar_tensor_tensor(dev[:, 1:2], dev[:, 0:1], dev[:, 0:1], mv[:, 1:2], ALU.mult,
                                     ALU.add).then_inc(s["gn"], 1)
            dve.wait_ge(s["gn_mm"], START + b * 2 + 2)
            dve.tensor_copy(dev[:, 2:3], pg[:, 0:1]).then_inc(s["gn"], 1)
            dve.wait_ge(s["gn_sqrt"], START + b + 1)
            dve.reciprocal(dev[:, 4:5], dev[:, 3:4]).then_inc(s["gn"], 1)
            dve.wait_ge(s["gn"], START + b * 5 + 5)
            dve.wait_ge(s["padded"], START + b + 1)
            dve.tensor_scalar(padded[:, 1:1 + H, 1:1 + W], x_ch[:, :].rearrange("p (i j) -> p i j", j=W),
                              dev[:, 5:6], dev[:, 4:5], ALU.subtract, ALU.mult).then_inc(s["normed"], 1)


SCAN_SEMAPHORES = [
    "b_wide", "b_kept", "c_wide", "decay", "drive", "scanned", "read_out", "summed", "carried", "y_added",
    "projected", "xd_kept", "first_part", "rest1", "second_part", "parts", "step_mm", "step_abs",
    "step_exp", "step_ln", "step", "step_u", "y_begun",
]


def scan_semaphores(nc, ctx):
    return {n: ctx.enter_context(nc.semaphore("s_" + n)) for n in SCAN_SEMAPHORES}


class Chunk:

    def __init__(self, b, k, i, place, parity, first=False, last=False):
        self.k, self.parity, self.first, self.last = k, parity, first, last
        self.g = b * (NK * NCH) + (i + k * NCH)
        self.q = b * (NK * NCH * NS) + (i * NS + k * NCH * NS)
        self.carry = b * (NK * (NCH - 1) * NS) + (i * NS + k * (NCH - 1) * NS)
        self.start = place == 0
        self.end = place == NCH - 1
        self.backward = k >= 2
        self.at = (i * -L + (NCH - 1) * L) if self.backward else i * L


def chunk_stream(eng, b, body):
    for k in range(NK):
        after = Chunk(b, k + 1, 0, 0, 0) if k + 1 < NK else None
        head = Chunk(b, k, 0, 0, 0, first=k == 0)
        tail = Chunk(b, k, NCH - 1, NCH - 1, 1, last=k == NK - 1)
        body(head, Chunk(b, k, 1, 1, 1))
        with eng.Fori(0, (NCH - 2) // 2) as j:
            odd, even = (Chunk(b, k, j * 2 + 1, 1, 1), Chunk(b, k, j * 2 + 2, 2, 0))
            body(odd, even)
            body(even, Chunk(b, k, j * 2 + 3, 3, 1))
        body(tail, after)


def scans(nc, m, b):
    s = m.sem_b
    with ExitStack() as ctx:
        sb = lambda n, sh, d=fp32: ctx.enter_context(nc.sbuf_tensor(n, sh, d))
        ps = lambda n, sh: ctx.enter_context(nc.psum_tensor(n, sh, fp32))
        xd = sb("xd", [P, L])
        part0 = sb("part0", [P, L], bf16)
        rest = sb("rest", [P, L])
        part1 = sb("part1", [P, L], bf16)
        parts = sb("parts", [P, 2, L], bf16)
        softplus = sb("softplus", [P, DT2, L])
        step = sb("step", [P, 2, DT2, L])
        step_u = sb("step_u", [P, 2, DT2, L])
        b_kept = sb("b_kept", [P, 4, L])
        state = sb("state", [P, 4, DT2, L])
        read = sb("read", [P, 4, DT2, L])
        carry = sb("carry", [P, NS, DT2])
        p_prep = ps("p_prep", [P, L])
        p_b = ps("p_b", [P, L])
        p_c = ps("p_c", [P, 2, L])
        p_decay = ps("p_decay", [P, DT2, L])
        p_y = ps("p_y", [P, DT2, L])
        block = ctx.enter_context(nc.Block())

        def u_of(c):
            return (m.s1 if c.k % 2 == 0 else m.s2)[:, :, ds(c.at, L)]

        def flip(ap, c):
            return ap[:, ::-1] if c.backward else ap

        @block.tensor
        def _(pe):
            def project(c):
                pe.wait_ge(s["step_abs"], START + c.g * 2)
                for t in range(DT2):
                    last = pe.matmul(p_prep[:, :], m.xproj[:, DT2 * c.k + t, :], u_of(c)[:, t, :],
                                     start=t == 0, stop=t == DT2 - 1)
                last.then_inc(s["projected"], 1)

            def step_product(c, t):
                if t == 0:
                    pe.wait_ge(s["xd_kept"], START + c.g + 1)
                else:
                    pe.wait_ge(s["step_abs"], START + c.g * 2 + 1)
                pe.matmul(p_prep[:, :], m.w_dt[0:NR, DT2 * c.k + t, :], xd[0:NR, :], start=True,
                          stop=True).then_inc(s["step_mm"], 1)

            def widen_b(c, n):
                if n == 0:
                    pe.wait_ge(s["parts"], START + c.g + 1)
                pe.wait_ge(s["b_kept"], START + c.q + n)
                pe.matmul(p_b[:, :], m.select[:, n, :], parts[:, c.parity, :], start=True,
                          stop=True).then_inc(s["b_wide"], 1)

            def widen_c(c, n):
                if not (c.first and n < 2):
                    pe.wait_ge(s["read_out"], START + c.q + (n - 1))
                pe.matmul(p_c[:, n % 2, :], m.select[:, NS + n, :], parts[:, c.parity, :], start=True,
                          stop=True).then_inc(s["c_wide"], 1)

            def body(c, nxt):
                if c.first:
                    project(c)
                    step_product(c, 0)
                    step_product(c, 1)
                    for n in range(4):
                        widen_b(c, n)
                    widen_c(c, 0)
                for n in range(NS):
                    if nxt and n == 0:
                        project(nxt)
                    if nxt and n in (4, 7):
                        step_product(nxt, n // 6)
                    if n + 4 < NS:
                        widen_b(c, n + 4)
                    elif nxt:
                        widen_b(nxt, n + 4 - NS)
                    if n + 1 < NS:
                        widen_c(c, n + 1)
                    elif nxt:
                        widen_c(nxt, 0)
                    if n == 0:
                        pe.wait_ge(s["y_added"], START + c.g)
                    pe.wait_ge(s["read_out"], START + c.q + (n + 1))
                    for t in range(DT2):
                        last = pe.matmul(p_y[:, t, :], m.ident[:, :], read[:, n % 4, t, :], start=n == 0,
                                         stop=n == NS - 1)
                    last.then_inc(s["summed"], 1)

            chunk_stream(pe, b, body)

        @block.scalar
        def _(act):
            def keep_projection(c):
                act.wait_ge(s["projected"], START + c.g + 1)
                act.wait_ge(s["rest1"], START + c.g)
                act.wait_ge(s["step_mm"], START + c.g * 2)
                act.copy(xd[:, :], p_prep[:, :]).then_inc(s["xd_kept"], 1)

            def first_part(c):
                act.wait_ge(s["xd_kept"], START + c.g + 1)
                act.copy(part0[:, :], xd[:, :]).then_inc(s["first_part"], 1)

            def second_part(c):
                act.wait_ge(s["rest1"], START + c.g + 1)
                act.wait_ge(s["parts"], START + c.g)
                act.copy(part1[:, :], rest[:, :]).then_inc(s["second_part"], 1)

            def step_bias(c, t):
                act.wait_ge(s["step_mm"], START + c.g * 2 + (t + 1))
                act.wait_ge(s["step"], START + c.g)
                bias = m.dt_b[:, DT2 * c.k + t:DT2 * c.k + t + 1]
                act.activation(softplus[:, t, :], p_prep[:, :], ACT.Abs, bias=bias)
                act.activation(step[:, c.parity, t, :], p_prep[:, :], ACT.Relu, bias=bias).then_inc(s["step_abs"], 1)

            def step_exp(c):
                act.wait_ge(s["step_abs"], START + c.g * 2 + 2)
                act.activation(softplus[:, :, :], softplus[:, :, :], ACT.Exp, scale=-1.0).then_inc(s["step_exp"], 1)

            def step_ln(c):
                act.wait_ge(s["step_exp"], START + c.g + 1)
                act.activation(softplus[:, :, :], softplus[:, :, :], ACT.Ln, bias=1.0).then_inc(s["step_ln"], 1)

            def keep_b(c, n):
                act.wait_ge(s["b_wide"], START + c.q + (n + 1))
                if not (c.first and n < 4):
                    act.wait_ge(s["drive"], START + c.q + (n - 3))
                act.copy(b_kept[:, n % 4, :], p_b[:, :]).then_inc(s["b_kept"], 1)

            def decay(c, n):
                if n == 0:
                    act.wait_ge(s["step"], START + c.g + 1)
                for t in range(DT2):
                    if not (c.first and n == 0):
                        act.wait_ge(s["scanned"], START + c.q * 2 + (2 * n + t - 1))
                    act.activation(p_decay[:, t, :], step[:, c.parity, t, :], ACT.Exp,
                                   scale=m.a_neg[:, DT2 * c.k + t, n:n + 1]).then_inc(s["decay"], 1)

            def carry_on(c, n):
                act.wait_ge(s["scanned"], START + c.q * 2 + (2 * n + 2))
                end = 0 if c.backward else L - 1
                act.copy(carry[:, n, :], state[:, n % 4, :, end]).then_inc(s["carried"], 1)

            preparation = {3: keep_projection, 4: first_part, 6: lambda c: step_bias(c, 0), 7: second_part,
                           9: lambda c: step_bias(c, 1), 10: step_exp, 11: step_ln}

            def body(c, nxt):
                if c.first:
                    for n in sorted(preparation):
                        preparation[n](c)
                    keep_b(c, 0)
                    keep_b(c, 1)
                for n in range(NS):
                    decay(c, n)
                    if n + 2 < NS:
                        keep_b(c, n + 2)
                    elif nxt:
                        keep_b(nxt, n + 2 - NS)
                    if nxt and n in preparation:
                        preparation[n](nxt)
                    if not c.end and n:
                        carry_on(c, n - 1)
                if not c.end:
                    carry_on(c, NS - 1)

            chunk_stream(act, b, body)

        @block.gpsimd
        def _(pool):
            def step_times_u(c):
                pool.wait_ge(s["step"], START + c.g + 1)
                pool.tensor_tensor(step_u[:, c.parity, :, :], step[:, c.parity, :, :], u_of(c),
                                   ALU.mult).then_inc(s["step_u"], 1)

            def body(c, nxt):
                if c.first:
                    step_times_u(c)
                for n in range(NS):
                    if n == 0:
                        pool.wait_ge(s["step_u"], START + c.g + 1)
                    pool.wait_ge(s["b_kept"], START + c.q + (n + 1))
                    if not (c.first and n < 4):
                        pool.wait_ge(s["read_out"], START + c.q + (n - 3))
                        if n >= 4 and not c.end:
                            pool.wait_ge(s["carried"], START + c.carry + (n - 3))
                        if n < 4 and not c.start:
                            pool.wait_ge(s["carried"], START + c.carry + (n - 3))
                    wide = b_kept[:, n % 4, :].unsqueeze(1).broadcast_to([P, DT2, L])
                    pool.tensor_tensor(state[:, n % 4, :, :], step_u[:, c.parity, :, :], wide,
                                       ALU.mult).then_inc(s["drive"], 1)
                    if nxt and n == 14:
                        step_times_u(nxt)

            chunk_stream(pool, b, body)

        @block.vector
        def _(dve):
            def rest_of_first(c):
                dve.wait_ge(s["first_part"], START + c.g + 1)
                dve.scalar_tensor_tensor(rest[:, :], part0[:, :], m.part_mask[:, 0:1], xd[:, :], ALU.mult,
                                         ALU.add).then_inc(s["rest1"], 1)

            def third_part(c):
                dve.wait_ge(s["second_part"], START + c.g + 1)
                dve.wait_ge(s["rest1"], START + c.g + 1)
                if not c.first:
                    dve.wait_ge(s["c_wide"], START + c.q + (-NS))
                dve.scalar_tensor_tensor(parts[:, c.parity, :], part1[:, :], m.part_mask[:, 1:2], rest[:, :],
                                         ALU.mult, ALU.add).then_inc(s["parts"], 1)

            def finish_step(c):
                dve.wait_ge(s["step_ln"], START + c.g + 1)
                dve.tensor_tensor(step[:, c.parity, :, :], step[:, c.parity, :, :], softplus[:, :, :],
                                  ALU.add).then_inc(s["step"], 1)

            def add_y(c):
                dve.wait_ge(s["summed"], START + c.q + NS)
                dve.wait_ge(s["y_added"], START + c.g)
                if c.k % 2 == 0:
                    y, p = m.y[:, :, ds(c.at, L)], p_y[:, :, :]
                else:
                    column = (c.at // W)
                    y = m.y[:, :, :].rearrange("p t (h w) -> p t w h", w=W)[:, :, ds(column, L // H), :]
                    p = p_y[:, :, :].rearrange("p t (w h) -> p t w h", h=H)
                dve.tensor_tensor(y, y, p, ALU.add).then_inc(s["y_added"], 1)

            def scan(c, n):
                dve.wait_ge(s["drive"], START + c.q + (n + 1))
                if not c.start:
                    dve.wait_ge(s["carried"], START + c.carry + (n + 1 - NS))
                for t in range(DT2):
                    dve.wait_ge(s["decay"], START + c.q * 2 + (2 * n + t + 1))
                    h = flip(state[:, n % 4, t, :], c)
                    dve.tensor_tensor_scan(h, flip(p_decay[:, t, :], c), h,
                                           0.0 if c.start else carry[:, n, t:t + 1], ALU.mult,
                                           ALU.add).then_inc(s["scanned"], 1)

            def times_c(c, n):
                dve.wait_ge(s["scanned"], START + c.q * 2 + (2 * n + 2))
                dve.wait_ge(s["c_wide"], START + c.q + (n + 1))
                if not (c.first and n < 4):
                    dve.wait_ge(s["summed"], START + c.q + (n - 3))
                wide = p_c[:, n % 2, :].unsqueeze(1).broadcast_to([P, DT2, L])
                dve.tensor_tensor(read[:, n % 4, :, :], state[:, n % 4, :, :], wide,
                                  ALU.mult).then_inc(s["read_out"], 1)

            before = [None]

            def body(c, nxt):
                if c.first:
                    rest_of_first(c)
                    third_part(c)
                    finish_step(c)
                    for t in range(DT2):
                        dve.tensor_scalar(m.y[:, t, :], m.s1[:, t, :], m.d_skip[:, 8 + t:9 + t], None,
                                          ALU.mult).then_inc(s["y_begun"], 1)
                    dve.wait_ge(s["y_begun"], START + b * 4 + 2)
                    for t in range(DT2):
                        y = m.y[:, t, :].rearrange("p (h w) -> p w h", w=W)
                        dve.scalar_tensor_tensor(y, m.s2[:, t, :].rearrange("p (w h) -> p w h", h=H),
                                                 m.d_skip[:, 10 + t:11 + t], y, ALU.mult,
                                                 ALU.add).then_inc(s["y_begun"], 1)
                    dve.wait_ge(s["y_begun"], START + b * 4 + 4)
                for n in range(NS):
                    scan(c, n)
                    if n:
                        times_c(c, n - 1)
                    elif not c.first:
                        times_c(Before(c), NS - 1)
                    if n == 1 and not c.first:
                        add_y(Before(c))
                    if nxt and n == 5:
                        rest_of_first(nxt)
                    if nxt and n == 8:
                        third_part(nxt)
                    if nxt and n == 12:
                        finish_step(nxt)
                if c.last:
                    times_c(c, NS - 1)
                    add_y(c)

            chunk_stream(dve, b, body)


class Before:

    def __init__(self, c):
        self.g, self.q, self.first = c.g + -1, c.q + -NS, False
        self.k = c.k - 1 if c.start else c.k
        backward = self.k >= 2
        if c.start:
            self.at = 0 if backward else (NCH - 1) * L
        else:
            self.at = c.at + (L if backward else -L)


OUT_SEMAPHORES = [
    "mean", "centred", "squared", "variance", "deviation", "inverse", "scaled", "affine", "gated", "product",
    "added", "in0", "in1", "out0", "out1",
]


def out_semaphores(nc, ctx):
    return {n: ctx.enter_context(nc.semaphore("o_" + n)) for n in OUT_SEMAPHORES}


def norm_and_project(nc, m, io, b):
    s = m.sem_c
    with ExitStack() as ctx:
        sb = lambda n, sh, d=fp32: ctx.enter_context(nc.sbuf_tensor(n, sh, d))
        ps = lambda n, sh: ctx.enter_context(nc.psum_tensor(n, sh, fp32))
        gate = sb("gate_in", [P, 2, DT2, L])
        x_in = sb("x_in", [P, 2, 4, C])
        centred = sb("centred", [P, 2, DT2, L])
        work = sb("work", [P, 2, DT2, L])
        inv = sb("inv", [P, 2, L])
        t_out = sb("t_out", [P, 2, 4, C])
        p_mean = ps("p_mean", [P, 2, L])
        p_var = ps("p_var", [P, 2, L])
        p_out = ps("p_out", [P, 2, 4, C])
        block = ctx.enter_context(nc.Block())
        N2 = NCH // 2

        def tokens(dram, j, par):
            return dram[ds(b, 1), ds(j * 2 * L + par * L, L), :].rearrange("b (t p) c -> p (b t) c", p=P)

        @block.sync
        def _(sp):
            with sp.Fori(0, N2) as j:
                for par in range(2):
                    sp.wait_ge(s["added"], START + b * NCH + j * 2)
                    sp.dma_start(gate[:, par, :, :],
                                 m.gate_dram[ds(b, 1), :, :, ds(j * 2 * L + par * L, L)].rearrange("b p t l -> (b p) t l")
                                 ).then_inc(s[f"in{par}"], 16)
                    sp.dma_start(x_in[:, par, :, :], tokens(io["x"], j, par)).then_inc(s[f"in{par}"], 16)
                for par in range(2):
                    sp.wait_ge(s["added"], START + b * NCH + (j * 2 + (par + 1)))
                    sp.dma_start(tokens(m.t_dram, j, par), t_out[:, par, :, :]).then_inc(s[f"out{par}"], 16)

        @block.tensor
        def _(pe):
            with pe.Fori(0, N2) as j:
                n0 = b * NCH + j * 2
                for par in range(2):
                    pe.wait_ge(s["centred"], START + n0)
                    for t in range(DT2):
                        last = pe.matmul(p_mean[:, par, :], m.mean256[:, :], m.y[:, t, ds(j * 2 * L + par * L, L)],
                                         start=t == 0, stop=t == DT2 - 1)
                    last.then_inc(s["mean"], 1)
                for par in range(2):
                    pe.wait_ge(s["squared"], START + n0 + (par + 1))
                    for t in range(DT2):
                        last = pe.matmul(p_var[:, par, :], m.mean256[:, :], work[:, par, t, :],
                                         start=t == 0, stop=t == DT2 - 1)
                    last.then_inc(s["variance"], 1)
                for par in range(2):
                    pe.wait_ge(s["gated"], START + n0 + (par + 1))
                    for i in range(4):
                        for t in range(DT2):
                            last = pe.matmul(p_out[:, par, i, :], work[:, par, t, i * P:i * P + P], m.w_o[:, t, :],
                                             start=t == 0, stop=t == DT2 - 1)
                    last.then_inc(s["product"], 1)

        @block.scalar
        def _(act):
            with act.Fori(0, N2) as j:
                n0 = b * NCH + j * 2
                for par in range(2):
                    act.wait_ge(s["centred"], START + n0 + (par + 1))
                    act.wait_ge(s["product"], START + n0)
                    act.activation(work[:, par, :, :], centred[:, par, :, :], ACT.Square).then_inc(s["squared"], 1)
                for par in range(2):
                    act.wait_ge(s["variance"], START + n0 + (par + 1))
                    act.activation(inv[:, par, :], p_var[:, par, :], ACT.Sqrt,
                                   bias=m.eps[:, 0:1]).then_inc(s["deviation"], 1)
                for par in range(2):
                    act.wait_ge(s["scaled"], START + n0 + (par + 1))
                    for t in range(DT2):
                        last = act.activation(work[:, par, t, :], centred[:, par, t, :], ACT.Identity,
                                              bias=m.ln_b[:, t:t + 1], scale=m.ln_w[:, t:t + 1])
                    last.then_inc(s["affine"], 1)

        @block.gpsimd
        def _(pool):
            with pool.Fori(0, N2) as j:
                n0 = b * NCH + j * 2
                for par in range(2):
                    pool.wait_ge(s["affine"], START + n0 + (par + 1))
                    pool.wait_ge(s[f"in{par}"], START + b * (32 * N2) + (j * 32 + 32))
                    pool.tensor_tensor(work[:, par, :, :], work[:, par, :, :], gate[:, par, :, :],
                                       ALU.mult).then_inc(s["gated"], 1)
            for par in range(2):
                pool.wait_ge(s[f"out{par}"], START + (b + 1) * (16 * N2))

        @block.vector
        def _(dve):
            with dve.Fori(0, N2) as j:
                n0 = b * NCH + j * 2
                for par in range(2):
                    dve.wait_ge(s["mean"], START + n0 + (par + 1))
                    dve.wait_ge(s["affine"], START + n0)
                    dve.tensor_tensor(centred[:, par, :, :], m.y[:, :, ds(j * 2 * L + par * L, L)],
                                      p_mean[:, par, :].unsqueeze(1).broadcast_to([P, DT2, L]),
                                      ALU.subtract).then_inc(s["centred"], 1)
                for par in range(2):
                    dve.wait_ge(s["deviation"], START + n0 + (par + 1))
                    dve.reciprocal(inv[:, par, :], inv[:, par, :]).then_inc(s["inverse"], 1)
                    dve.wait_ge(s["inverse"], START + n0 + (par + 1))
                    dve.tensor_tensor(centred[:, par, :, :], centred[:, par, :, :],
                                      inv[:, par, :].unsqueeze(1).broadcast_to([P, DT2, L]),
                                      ALU.mult).then_inc(s["scaled"], 1)
                for par in range(2):
                    dve.wait_ge(s["product"], START + n0 + (par + 1))
                    dve.wait_ge(s[f"in{par}"], START + b * (32 * N2) + (j * 32 + 32))
                    dve.wait_ge(s[f"out{par}"], START + b * (16 * N2) + j * 16)
                    dve.tensor_tensor(t_out[:, par, :, :], x_in[:, par, :, :], p_out[:, par, :, :],
                                      ALU.add).then_inc(s["added"], 1)


def attention(nc, m, t_out_dram):
    NBLK = T // L
    with ExitStack() as ctx:
        sb = lambda n, sh, d=fp32: ctx.enter_context(nc.sbuf_tensor(n, sh, d))
        ps = lambda n, sh: ctx.enter_context(nc.psum_tensor(n, sh, fp32))
        sem = lambda n: ctx.enter_context(nc.semaphore("t_" + n))
        t_in = sb("t_in", [P, NB, 4, C])
        normed = sb("t_normed", [P, NB, 4, C])
        stats = sb("t_stats", [P, NB, 4, 6])
        mv = sb("t_mv", [P, NB, 4, 2])
        rstd = sb("t_rstd", [P, NB, 4])
        n_ch = sb("t_nch", [P, NB, L])
        qk_min = sb("qk_min", [P, NB, 2, L])
        qk = sb("qk", [P, NB, 2, L])
        k_tok = sb("k_tok", [P, NB, 4, C])
        v_one = sb("v_one", [P, NB, 4, C + 2])
        kv = sb("kv", [P, NB, C + 2])
        score = sb("score", [P, NB, P])
        den = sb("den", [P, NB, 4])
        res = sb("t_res", [P, NB, 4, C])
        pa = [ps(f"pa{b}", [P, L]) for b in range(NB)]
        pq = [ps(f"pq{b}", [P, L]) for b in range(NB)]
        psc = [ps(f"psc{b}", [P, L]) for b in range(NB)]
        pn = [ps(f"pn{b}", [P, L]) for b in range(NB)]
        names = ["in0", "in1", "out0", "out1", "stats", "mv", "sd", "rstd", "normed", "turned", "n_ch", "qk_mm",
                 "qk_min", "qk_exp", "qk", "v_mm", "v", "k_mm", "k", "score_mm", "score", "num_mm", "kv_mm", "kv",
                 "den", "res", "one", "qk_max"]
        s = {n: sem(n) for n in names}
        start_counts(nc, s.values())
        block = ctx.enter_context(nc.Block())


        @block.sync
        def _(sp):
            with sp.Fori(0, NBLK) as j:
                for b in range(NB):
                    sp.wait_ge(s["res"], START + j * NB * 4)
                    sp.dma_start(t_in[:, b, :, :], m.t_dram[b, ds(j * L, L), :].rearrange("(t p) c -> p t c", p=P)
                                 ).then_inc(s[f"in{b}"], 16)
                for b in range(NB):
                    sp.wait_ge(s["res"], START + j * (NB * 4) + (3 * NB + b + 1))
                    sp.dma_start(t_out_dram[b, ds(j * L, L), :].rearrange("(t p) c -> p t c", p=P), res[:, b, :, :]
                                 ).then_inc(s[f"out{b}"], 16)
            for b in range(NB):
                sp.wait_ge(s[f"out{b}"], START + 16 * NBLK)

        @block.tensor
        def _(pe):
            with pe.Fori(0, NBLK) as j:
                for b in range(NB):
                    pe.wait_ge(s["normed"], START + j * (NB * 4) + (4 * b + 4))
                    pe.wait_ge(s["v"], START + j * NB)
                    for i in range(4):
                        last = pe.transpose(pa[b][:, i * P:i * P + P], normed[:, b, i, :], m.ident[:, :])
                    last.then_inc(s["turned"], 1)
                for w in range(2):
                    for b in range(NB):
                        if w == 0:
                            pe.wait_ge(s["n_ch"], START + j * NB + (b + 1))
                            pe.wait_ge(s["k"], START + j * NB)
                        else:
                            pe.wait_ge(s["qk_max"], START + j * (NB * 2) + (b + 1))
                        pe.matmul(pq[b][:, :], m.w_attn[:, w, :], n_ch[:, b, :], start=True,
                                  stop=True).then_inc(s["qk_mm"], 1)
                for b in range(NB):
                    for i in range(4):
                        last = pe.matmul(pa[b][:, i * P:i * P + P], n_ch[:, b, i * P:i * P + P], m.w_attn[:, 2, :],
                                         start=True, stop=True)
                    last.then_inc(s["v_mm"], 1)
                for b in range(NB):
                    pe.wait_ge(s["qk"], START + j * (NB * 2) + (NB + b + 1))
                    for i in range(4):
                        last = pe.transpose(pq[b][:, i * P:i * P + P], qk[:, b, 1, i * P:i * P + P], m.ident[:, :])
                    last.then_inc(s["k_mm"], 1)
                for i in range(4):
                    for b in range(NB):
                        n = j * (NB * 4) + (NB * i + b)
                        cut = slice(i * P, i * P + P)
                        pe.wait_ge(s["kv"], START + n + (1 - NB) if i else j * (NB * 4))
                        pe.matmul(psc[b][:, 0:P], qk[:, b, 1, cut], qk[:, b, 0, cut], start=True,
                                  stop=True).then_inc(s["score_mm"], 1)
                        if i == 0:
                            pe.wait_ge(s["v"], START + j * NB + (b + 1))
                            pe.wait_ge(s["k"], START + j * NB + (b + 1))
                    for b in range(NB):
                        n = j * (NB * 4) + (NB * i + b)
                        cut = slice(i * P, i * P + P)
                        pe.wait_ge(s["res"], START + n + (1 - NB) if i else j * (NB * 4))
                        pe.matmul(pn[b][:, 0:C + 2], qk[:, b, 0, cut], kv[:, b, :], start=True, stop=False)
                        pe.wait_ge(s["score"], START + n + 1)
                        pe.matmul(pn[b][:, 0:C + 2], score[:, b, :], v_one[:, b, i, :], start=False,
                                  stop=True).then_inc(s["num_mm"], 1)
                        pe.matmul(psc[b][:, P:2 * P + 2], k_tok[:, b, i, :], v_one[:, b, i, :], start=True,
                                  stop=True).then_inc(s["kv_mm"], 1)

        @block.scalar
        def _(act):
            with act.Fori(0, NBLK) as j:
                for b in range(NB):
                    act.wait_ge(s["mv"], START + j * (NB * 4) + (4 * b + 4))
                    act.activation(rstd[:, b, :], mv[:, b, :, 1], ACT.Sqrt, bias=m.eps[:, 0:1]).then_inc(s["sd"], 1)
                for b in range(NB):
                    act.wait_ge(s["turned"], START + j * NB + (b + 1))
                    act.copy(n_ch[:, b, :], pa[b][:, :]).then_inc(s["n_ch"], 1)
                for w in range(2):
                    for b in range(NB):
                        act.wait_ge(s["qk_min"], START + j * (NB * 2) + (NB * w + b + 1))
                        act.activation(qk_min[:, b, w, :], qk_min[:, b, w, :], ACT.Exp).then_inc(s["qk_exp"], 1)
                for b in range(NB):
                    act.wait_ge(s["k_mm"], START + j * NB + (b + 1))
                    act.copy(k_tok[:, b, :, :], pq[b][:, :].rearrange("p (i c) -> p i c", c=C)).then_inc(s["k"], 1)

        @block.gpsimd
        def _(pool):
            pool.memset(v_one[:, :, :, C:C + 1], 1.0).then_inc(s["one"], 1)
            pool.memset(v_one[:, :, :, C + 1:C + 2], 0.0).then_inc(s["one"], 1)
            pool.memset(kv[:, :, :], 0.0).then_inc(s["one"], 1)

        @block.vector
        def _(dve):
            dve.wait_ge(s["one"], START + 3)
            with dve.Fori(0, NBLK) as j:
                for b in range(NB):
                    dve.wait_ge(s[f"in{b}"], START + j * 16 + 16)
                    for i in range(4):
                        dve.bn_stats(stats[:, b, i, :], t_in[:, b, i, :]).then_inc(s["stats"], 1)
                for b in range(NB):
                    dve.wait_ge(s["stats"], START + j * (NB * 4) + (4 * b + 4))
                    dve.memset(m.idle[:, b:b + 1], 0.0)
                    for i in range(4):
                        dve.bn_aggr(mv[:, b, i, :], stats[:, b, i, :]).then_inc(s["mv"], 1)
                for b in range(NB):
                    dve.wait_ge(s["sd"], START + j * NB + (b + 1))
                    dve.reciprocal(rstd[:, b, :], rstd[:, b, :]).then_inc(s["rstd"], 1)
                for b in range(NB):
                    dve.wait_ge(s["rstd"], START + j * NB + (b + 1))
                    for i in range(4):
                        dve.tensor_scalar(normed[:, b, i, :], t_in[:, b, i, :], mv[:, b, i, 0:1],
                                          rstd[:, b, i:i + 1], ALU.subtract, ALU.mult).then_inc(s["normed"], 1)
                for w in range(2):
                    for b in range(NB):
                        n = j * (NB * 2) + (NB * w + b + 1)
                        dve.wait_ge(s["qk_mm"], START + n)
                        dve.tensor_scalar(qk_min[:, b, w, :], pq[b][:, :], m.b_qkv[:, w:w + 1], 0.0, ALU.add,
                                          ALU.min).then_inc(s["qk_min"], 1)
                        dve.tensor_scalar(qk[:, b, w, :], pq[b][:, :], m.b_qkv[:, w:w + 1], 0.0, ALU.add,
                                          ALU.max).then_inc(s["qk_max"], 1)
                for b in range(NB):
                    dve.wait_ge(s["v_mm"], START + j * NB + (b + 1))
                    dve.tensor_tensor(v_one[:, b, :, 0:C], pa[b][:, :].rearrange("p (i c) -> p i c", c=C),
                                      m.b_v[:, :].unsqueeze(1).broadcast_to([P, 4, C]), ALU.add).then_inc(s["v"], 1)
                for w in range(2):
                    for b in range(NB):
                        n = j * (NB * 2) + (NB * w + b + 1)
                        dve.wait_ge(s["qk_exp"], START + n)
                        dve.wait_ge(s["qk_max"], START + n)
                        dve.tensor_tensor(qk[:, b, w, :], qk[:, b, w, :], qk_min[:, b, w, :],
                                          ALU.add).then_inc(s["qk"], 1)
                for b in range(NB):
                    dve.wait_ge(s[f"out{b}"], START + j * 16)
                for i in range(4):
                    for b in range(NB):
                        n = j * (NB * 4) + (NB * i + b)
                        dve.wait_ge(s["score_mm"], START + n + 1)
                        dve.tensor_tensor(score[:, b, :], psc[b][:, 0:P], m.causal[:, :],
                                          ALU.mult).then_inc(s["score"], 1)
                    for b in range(NB):
                        n = j * (NB * 4) + (NB * i + b)
                        dve.wait_ge(s["kv_mm"], START + n + 1)
                        dve.tensor_tensor(kv[:, b, :], kv[:, b, :], psc[b][:, P:2 * P + 2],
                                          ALU.add).then_inc(s["kv"], 1)
                    for b in range(NB):
                        dve.tensor_scalar(den[:, b, 0:1], pn[b][:, C:C + 1], 1e-6, None, ALU.add).then_inc(s["den"], 1)
                    for b in range(NB):
                        dve.wait_ge(s["den"], START + j * (NB * 8) + (NB * 2 * i + b + 1))
                        dve.reciprocal(den[:, b, 1:2], den[:, b, 0:1]).then_inc(s["den"], 1)
                    for b in range(NB):
                        dve.wait_ge(s["den"], START + j * (NB * 8) + (NB * 2 * i + NB + b + 1))
                        dve.scalar_tensor_tensor(res[:, b, i, :], pn[b][:, 0:C], den[:, b, 1:2], t_in[:, b, i, :],
                                                 ALU.mult, ALU.add).then_inc(s["res"], 1)


KF, LAGS, FRACS = 16, 3, 4
HALF = T // 2
PAD = P
TARGETS = [(1536, 512, 1), (1024, 512, 1), (512, 512, 2), (256, 256, 3), (0, 256, 4)]


def filters_and_weights(nc, m, io):
    with ExitStack() as ctx:
        sb = lambda n, sh, d=fp32: ctx.enter_context(nc.sbuf_tensor(n, sh, d))
        sem = lambda n: ctx.enter_context(nc.semaphore("f_" + n))
        phi = sb("phi", [P, 32, KF])
        taps = sb("taps", [KF, 2, HALF])
        high = sb("taps_high", [KF, 2, HALF], fp32r)
        low = sb("taps_low", [KF, 2, HALF], fp32r)
        zero = sb("taps_zero", [KF, 2, PAD])
        lw = sb("lw", [P, 2, FRACS])
        sig = sb("sig", [P, KF])
        wk = sb("wk", [P, 8, FRACS])
        pt = [ctx.enter_context(nc.psum_tensor(f"fpt{i}", [KF, 512], fp32)) for i in range(8)]
        loaded, turned, kept, split = sem("loaded"), sem("turned"), sem("kept"), sem("split")
        soft, root, stored, zeroed = sem("soft"), sem("root"), sem("stored"), sem("zeroed")
        block = ctx.enter_context(nc.Block())

        @block.sync
        def _(sp):
            sp.dma_start(phi[:, :, :], io["phi"].rearrange("(p r) k -> p r k", r=32)).then_inc(loaded, 16)
            sp.dma_start(lw[:, 0, :], io["log_w"].partition_broadcast(P)).then_inc(loaded, 16)
            sp.dma_start(lw[:, 1, :], io["gumbel"].partition_broadcast(P)).then_inc(loaded, 16)
            sp.dma_start(sig[:, :], io["sigma"].partition_broadcast(P)).then_inc(loaded, 16)
            sp.wait_ge(zeroed, 1)
            sp.wait_ge(split, 2)
            for part, src in enumerate((high, low)):
                sp.dma_start(m.taps_dram[part, :, :, HALF:HALF + PAD], zero[:, :, :]).then_inc(stored, 16)
                sp.dma_start(m.taps_dram[part, :, :, 0:HALF], src[:, :, :].bitcast(fp32)).then_inc(stored, 16)
            sp.wait_ge(stored, 64)

        @block.tensor
        def _(pe):
            pe.wait_ge(loaded, 64)
            for r in range(32):
                last = pe.transpose(pt[r // 4][:, (r % 4) * P:(r % 4) * P + P], phi[:, r, :], m.ident[:, :])
                if r % 4 == 3:
                    last.then_inc(turned, 1)

        @block.scalar
        def _(act):
            act.wait_ge(soft, 3)
            act.activation(wk[:, 1, :], wk[:, 0, :], ACT.Exp, bias=wk[:, 7, 1:2]).then_inc(root, 1)
            act.wait_ge(loaded, 64)
            act.activation(sig[:, :], sig[:, :], ACT.Sqrt).then_inc(root, 1)
            act.wait_ge(root, 2)
            act.activation(sig[:, :], sig[:, :], ACT.Sqrt).then_inc(root, 1)

        @block.vector
        def _(dve):
            n = [0]

            def then(ins):
                n[0] += 1
                ins.then_inc(soft, 1)
                dve.wait_ge(soft, n[0])

            X = mybir.AxisListType.X
            dve.memset(zero[:, :, :], 0.0).then_inc(zeroed, 1)
            dve.wait_ge(loaded, 64)
            then(dve.tensor_tensor(wk[:, 0, :], lw[:, 0, :], lw[:, 1, :], ALU.add))
            then(dve.tensor_reduce(wk[:, 7, 0:1], wk[:, 0, :], axis=X, op=ALU.max))
            then(dve.tensor_scalar(wk[:, 7, 1:2], wk[:, 7, 0:1], -1.0, None, ALU.mult))
            dve.wait_ge(root, 1)
            then(dve.tensor_reduce(wk[:, 7, 2:3], wk[:, 1, :], axis=X, op=ALU.add))
            then(dve.reciprocal(wk[:, 7, 3:4], wk[:, 7, 2:3]))
            then(dve.tensor_scalar(wk[:, 2, :], wk[:, 1, :], wk[:, 7, 3:4], None, ALU.mult))
            then(dve.tensor_reduce(wk[:, 6, 0:1], wk[:, 2, :], axis=X, op=ALU.max))
            then(dve.tensor_scalar(wk[:, 3, :], wk[:, 2, :], wk[:, 6, 0:1], None, ALU.is_equal))
            then(dve.memset(wk[:, 4, 0:1], 0.0))
            for i in range(1, FRACS):
                then(dve.tensor_tensor(wk[:, 4, i:i + 1], wk[:, 4, i - 1:i], wk[:, 3, i - 1:i], ALU.max))
            then(dve.tensor_tensor(wk[:, 5, :], wk[:, 3, :], wk[:, 4, :], ALU.is_gt))
            then(dve.tensor_tensor(wk[:, 5, :], wk[:, 5, :], wk[:, 2, :], ALU.subtract))
            then(dve.tensor_tensor(m.frac_w[:, :], wk[:, 5, :], wk[:, 2, :], ALU.add))
            dve.wait_ge(root, 3)
            for i in range(FRACS):
                then(dve.tensor_scalar(m.frac_filter[:, i, :], sig[:, :], m.frac_w[:, i:i + 1], None, ALU.mult))
            for i in range(8):
                dve.wait_ge(turned, i + 1)
                for par in range(2):
                    dst = taps[:, par, :].rearrange("k (p h) -> k h p", h=16)[:, 14 - 2 * i:16 - 2 * i, :][:, ::-1, ::-1]
                    src = pt[i][:, :].rearrange("k (h two p) -> k two h p", two=2, h=2)[:, par, :, :]
                    dve.tensor_copy(dst, src).then_inc(kept, 1)
            dve.wait_ge(kept, 16)
            dve.tensor_copy(high[:, :, :], taps[:, :, :]).then_inc(split, 1)
            dve.wait_ge(split, 1)
            dve.tensor_tensor(low[:, :, :], taps[:, :, :], high[:, :, :].bitcast(fp32), ALU.subtract).then_inc(split, 1)


def sources(nc, m):
    NT = T // P
    with ExitStack() as ctx:
        sb = lambda n, sh, d=fp32: ctx.enter_context(nc.sbuf_tensor(n, sh, d))
        sem = lambda n: ctx.enter_context(nc.semaphore("u_" + n))
        u = sb("u_raw", [P, NT, C])
        stats = sb("u_stats", [P, NT, 6])
        mv = sb("u_mv", [P, NT, 2])
        rstd = sb("u_rstd", [P, NT])
        pt = [ctx.enter_context(nc.psum_tensor(f"upt{i}", [P, 512], fp32)) for i in range(4)]
        loaded, stat, agg, dev, inv = sem("loaded"), sem("stat"), sem("agg"), sem("dev"), sem("inv")
        normed, high, low, turned, kept, zeroed = (sem("normed"), sem("high"), sem("low"), sem("turned"), sem("kept"),
                                                   sem("zeroed"))
        block = ctx.enter_context(nc.Block())

        @block.sync
        def _(sp):
            for b in range(NB):
                if b:
                    sp.wait_ge(low, b)
                    sp.wait_ge(turned, 8 * b)
                sp.dma_start(u[:, :, :].rearrange("p (j two) c -> p j two c", two=2),
                             m.t2_dram[b].rearrange("(j p two) c -> p j two c", two=2, p=P)).then_inc(loaded, 16)

        @block.scalar
        def _(act):
            for b in range(NB):
                act.wait_ge(agg, NT * (b + 1))
                act.activation(rstd[:, :], mv[:, :, 1], ACT.Sqrt, bias=m.eps[:, 0:1]).then_inc(dev, 1)
                for i in range(8):
                    act.wait_ge(turned, 8 * b + i + 1)
                    dst = m.u_t[:, b, :, 1 + 256 * i:1 + 256 * i + 256].rearrange("c two (j t) -> c j two t", j=2)
                    act.copy(dst, pt[i % 4][:, :].rearrange("c (j two t) -> c j two t", two=2, j=2)).then_inc(kept, 1)

        @block.vector
        def _(dve):
            dve.memset(m.u_t[:, :, :, 0:1], 0.0).then_inc(zeroed, 1)
            for b in range(NB):
                dve.wait_ge(loaded, 16 * (b + 1))
                for i in range(NT):
                    dve.bn_stats(stats[:, i, :], u[:, i, :]).then_inc(stat, 1)
                for i in range(NT):
                    dve.wait_ge(stat, NT * b + i + 1)
                    dve.bn_aggr(mv[:, i, :], stats[:, i, :]).then_inc(agg, 1)
                dve.wait_ge(dev, b + 1)
                dve.reciprocal(rstd[:, :], rstd[:, :]).then_inc(inv, 1)
                dve.wait_ge(inv, b + 1)
                for i in range(NT):
                    dve.tensor_scalar(u[:, i, :], u[:, i, :], mv[:, i, 0:1], rstd[:, i:i + 1], ALU.subtract,
                                      ALU.mult).then_inc(normed, 1)
                dve.wait_ge(normed, NT * (b + 1))
                dve.tensor_copy(m.u_high[:, b, :, :], u[:, :, :]).then_inc(high, 1)
                dve.wait_ge(high, b + 1)
                dve.tensor_tensor(m.u_low[:, b, :, :], u[:, :, :], m.u_high[:, b, :, :].bitcast(fp32),
                                  ALU.subtract).then_inc(low, 1)

        @block.tensor
        def _(pe):
            for b in range(NB):
                for i in range(8):
                    pe.wait_ge(normed, NT * b + 4 * i + 4)
                    if 8 * b + i >= 4:
                        pe.wait_ge(kept, 8 * b + i - 3)
                    for r in range(4):
                        last = pe.transpose(pt[i % 4][:, r * P:r * P + P], u[:, 4 * i + r, :], m.ident[:, :])
                    last.then_inc(turned, 1)


def spectral(nc, m, io, out):
    with ExitStack() as keep:
        sbk = lambda n, sh, d=fp32: keep.enter_context(nc.sbuf_tensor(n, sh, d))
        m.frac_w = sbk("frac_w", [P, FRACS])
        m.frac_filter = sbk("frac_filter", [P, FRACS, KF])
        m.taps_dram = nc.dram_tensor("taps_scratch", [2, KF, 2, PAD + HALF], fp32, kind="Internal").ap()
        filters_and_weights(nc, m, io)
        m.u_high = sbk("u_high", [P, NB, T // P, C], fp32r)
        m.u_low = sbk("u_low", [P, NB, T // P, C], fp32r)
        m.u_t = sbk("u_t", [P, NB, 2, 1 + HALF])
        sources(nc, m)
        with ExitStack() as ctx:
            sb = lambda n, sh, d=fp32: ctx.enter_context(nc.sbuf_tensor(n, sh, d))
            sem = lambda n: ctx.enter_context(nc.semaphore("c_" + n))
            shifted = [[sb(f"shifted{kind}{part}", [P, kind + HALF], fp32r) for part in range(2)] for kind in range(2)]
            mixing = sb("mixing", [P, 2, KF, C])
            mix_now = sb("mix_now", [P, 2, C])
            recur = sb("recur", [P, LAGS, C])
            m_plus, m_minus, m_sum = sb("m_plus", [P, KF, C]), sb("m_minus", [P, KF, C]), sb("m_sum", [P, KF, C])
            m_u = sb("m_u", [P, LAGS, C])
            filtered = sb("filtered", [P, 4, L])
            turned_out = sb("turned_out", [P, 4, L])
            t_in = sb("r_in", [P, 4, C])
            result = sb("result", [P, 2, 4, C])
            p_conv = [ctx.enter_context(nc.psum_tensor(f"p_conv{i}", [P, L], fp32)) for i in range(4)]
            p_mix = [ctx.enter_context(nc.psum_tensor(f"p_mix{i}", [P, L], fp32)) for i in range(4)]
            names = ["m_in", "m_sums", "m_zero", "mixing", "mix_now0", "mix_now1", "mixed0", "mixed1", "z0", "z1",
                     "conv0", "conv1", "filtered", "kept", "out_t", "added", "t_in",
                     "out0", "out1"]
            s = {n: sem(n) for n in names}
            start_counts(nc, s.values())
            block = ctx.enter_context(nc.Block())
            groups = [(b, par) for b in range(NB) for par in range(2)]
            NT = len(TARGETS)
            reach = [r for _, _, r in TARGETS]
            updates = [n for n in range(NT) if n == 0 or reach[n] != reach[n - 1]]

            def out_tokens(dram, b, par, t0, size):
                return dram[b].rearrange("(t p two) c -> p t two c", two=2, p=P)[:, t0 // P:(t0 + size) // P, par, :]

            @block.sync
            def _(sp):
                for n, (t0, size, _) in enumerate(TARGETS):
                    with sp.Fori(0, KF) as k:
                        for kind in range(2):
                            sp.wait_ge(s[f"conv{kind}"], START + k * 4 + 4 * KF * n)
                            for part in range(2):
                                width = t0 + size + kind
                                src = m.taps_dram[part][ds(k, 1), kind, :].rearrange("k x -> (k x)")
                                src = shifted_rows(src, HALF - (t0 + size), width)
                                sp.dma_start(shifted[kind][part][:, 0:width].bitcast(fp32), src).then_inc(s[f"z{kind}"], 16)

            @block.scalar
            def _(act):
                for i in range(FRACS):
                    if i:
                        act.wait_ge(s["mixing"], START + i)
                    act.dma_start(m_plus[:, :, :], io["M_plus"][i].rearrange("k d e -> d k e")).then_inc(s["m_in"], 16)
                    act.dma_start(m_minus[:, :, :], io["M_minus"][i].rearrange("k d e -> d k e")).then_inc(s["m_in"], 16)
                    act.dma_start(m_u[:, :, :], io["M_u"][i].rearrange("j d e -> d j e")).then_inc(s["m_in"], 16)
                    for n, (t0, size, r) in enumerate(TARGETS):
                        if r != i + 1:
                            continue
                        with act.Fori(0, KF) as k:
                            for g in range(8):
                                act.wait_ge(s[f"conv{g // 4}"], START + k * 4 + (4 * KF * n + g % 4 + 1))
                                of, count = ("mixed1", 0) if g == 0 else (f"mixed{(g - 1) // 4}", (g - 1) % 4 + 1)
                                act.wait_ge(s[of], START + k * 4 + (4 * KF * n + count))
                                act.copy(filtered[:, g % 4, 0:size], p_conv[g % 4][:, 0:size]).then_inc(s["filtered"], 1)
                        act.wait_ge(s["mixed1"], START + 4 * KF * (n + 1))
                        act.wait_ge(s["out_t"], START + 4 * n)
                        for g in range(4):
                            act.copy(turned_out[:, g, 0:size], p_mix[g][:, 0:size]).then_inc(s["kept"], 1)
                        for g, (b, par) in enumerate(groups):
                            act.wait_ge(s["added"], START + 4 * n + g)
                            act.dma_start(t_in[:, 0:size // P, :], out_tokens(m.t2_dram, b, par, t0, size)
                                          ).then_inc(s["t_in"], 16)
                            act.wait_ge(s["added"], START + 4 * n + g + 1)
                            act.dma_start(out_tokens(out, b, par, t0, size), result[:, g % 2, 0:size // P, :]
                                          ).then_inc(s[f"out{g % 2}"], 16)
                for i in range(2):
                    act.wait_ge(s[f"out{i}"], START + 16 * 2 * NT)

            @block.gpsimd
            def _(pool):
                for n in range(NT):
                    pool.wait_ge(s["mixing"], START + reach[n])
                    with pool.Fori(0, KF) as k:
                        for kind in range(2):
                            pool.wait_ge(s[f"mixed{kind}"], START + k * 4 + 4 * KF * n)
                            pool.tensor_copy(mix_now[:, kind, :], mixing[:, kind, ds(k, 1), :].rearrange("p k e -> p (k e)")
                                             ).then_inc(s[f"mix_now{kind}"], 1)

            @block.vector
            def _(dve):
                dve.memset(mixing[:, :, :, :], 0.0).then_inc(s["m_zero"], 1)
                dve.memset(recur[:, :, :], 0.0).then_inc(s["m_zero"], 1)
                dve.wait_ge(s["m_zero"], START + 2)
                i = 0
                for n, (t0, size, r) in enumerate(TARGETS):
                    if n in updates:
                        dve.wait_ge(s["m_in"], START + 48 * (i + 1))
                        if n:
                            for kind in range(2):
                                dve.wait_ge(s[f"mix_now{kind}"], START + KF * n)
                            dve.wait_ge(s["mixed1"], START + 4 * KF * n)
                        dve.tensor_tensor(m_sum[:, :, :], m_plus[:, :, :], m_minus[:, :, :], ALU.add).then_inc(s["m_sums"], 1)
                        dve.tensor_tensor(m_plus[:, :, :], m_plus[:, :, :], m_minus[:, :, :],
                                          ALU.subtract).then_inc(s["m_sums"], 1)
                        dve.wait_ge(s["m_sums"], START + 2 * i + 2)
                        for j in range(LAGS):
                            dve.scalar_tensor_tensor(recur[:, j, :], m_u[:, j, :], m.frac_w[:, i:i + 1], recur[:, j, :],
                                                     ALU.mult, ALU.add)
                        for k in range(KF):
                            for kind, src in ((0, m_sum), (1, m_plus)):
                                last = dve.scalar_tensor_tensor(mixing[:, kind, k, :], src[:, k, :],
                                                                m.frac_filter[:, i, k:k + 1], mixing[:, kind, k, :],
                                                                ALU.mult, ALU.add)
                        last.then_inc(s["mixing"], 1)
                        i += 1
                    for g in range(4):
                        dve.wait_ge(s["out_t"], START + 4 * n + g + 1)
                        dve.wait_ge(s["t_in"], START + 16 * (4 * n + g + 1))
                        if 4 * n + g >= 2:
                            dve.wait_ge(s[f"out{g % 2}"], START + 16 * ((4 * n + g) // 2))
                        dve.tensor_tensor(result[:, g % 2, 0:size // P, :], t_in[:, 0:size // P, :],
                                          p_conv[g][:, 0:size].rearrange("p (t c) -> p t c", c=C),
                                          ALU.add).then_inc(s["added"], 1)

            @block.tensor
            def _(pe):
                for n, (t0, size, r) in enumerate(TARGETS):
                    pe.wait_ge(s["mixing"], START + r)
                    pe.wait_ge(s["kept"], START + 4 * n)
                    for g, (b, par) in enumerate(groups):
                        for lag in range(LAGS):
                            source = (par + lag) % 2
                            back = (lag + 1 - par) // 2
                            pe.matmul(p_mix[g][:, 0:size], recur[:, lag, :],
                                      m.u_t[:, b, source, 1 + t0 - back:1 + t0 - back + size], start=lag == 0,
                                      stop=lag == LAGS - 1)
                    with pe.Fori(0, KF) as k:
                        def mix(g):
                            kind, (b, par) = g // 4, groups[g % 4]
                            pe.wait_ge(s["filtered"], START + k * 8 + (8 * KF * n + g + 1))
                            if g % 4 == 0:
                                pe.wait_ge(s[f"mix_now{kind}"], START + k + (KF * n + 1))
                            last = pe.matmul(p_mix[g % 4][:, 0:size], mix_now[:, kind, :], filtered[:, g % 4, 0:size],
                                             start=False, stop=True, skip_group_check=True)
                            last.then_inc(s[f"mixed{kind}"], 1)

                        for g in range(8):
                            kind, (b, par) = g // 4, groups[g % 4]
                            if g % 4 == 0:
                                pe.wait_ge(s[f"z{kind}"], START + k * 32 + (32 * KF * n + 32))
                            if n and g < 4:
                                pe.wait_ge(s["added"], START + 4 * n)
                            source = par ^ kind
                            shift = -1 if kind and not par else 0
                            blocks = range((t0 + size) // P)
                            for jb in blocks:
                                lo = max(t0, jb * P)
                                width = t0 + size - lo
                                col = (t0 + size) - (lo - jb * P + shift) - width
                                o = p_conv[g % 4][:, lo - t0:size]
                                for x, z in ((m.u_high, 0), (m.u_high, 1), (m.u_low, 0)):
                                    last = pe.matmul(o, x[:, b, 2 * jb + source, :], shifted[kind][z][:, col:col + width][:, ::-1],
                                                     start=jb == 0 and x is m.u_high and z == 0,
                                                     stop=jb == blocks[-1] and x is m.u_low)
                            last.then_inc(s[f"conv{kind}"], 1)
                            if g:
                                mix(g - 1)
                        mix(7)
                    for g in range(4):
                        pe.wait_ge(s["kept"], START + 4 * n + g + 1)
                        for i in range(size // P):
                            last = pe.transpose(p_conv[g][:, i * P:i * P + P], turned_out[:, g, i * P:i * P + P],
                                                m.ident[:, :])
                        last.then_inc(s["out_t"], 1)


def shifted_rows(row, first, width):
    return bass.AP(tensor=row.tensor, offset=row.offset + first, ap=[[1, P], [1, width]])


class Memory:
    pass


INPUTS = {
    "x": "x", "W_in": "L0_conv_W_in", "conv_w": "L0_conv_conv_w", "conv_b": "L0_conv_conv_b",
    "x_proj_w": "L0_conv_x_proj_w", "dt_proj_w": "L0_conv_dt_proj_w", "dt_proj_b": "L0_conv_dt_proj_b",
    "A_logs": "L0_conv_A_logs", "Ds": "L0_conv_Ds", "ln_w": "L0_conv_ln_w", "ln_b": "L0_conv_ln_b",
    "W_out": "L0_conv_W_out", "attn_W": "L1_attn_W", "attn_b": "L1_attn_b", "sigma": "L1_ffn_sigma",
    "phi": "L1_ffn_phi", "M_u": "L1_ffn_M_u", "M_plus": "L1_ffn_M_phi_plus",
    "M_minus": "L1_ffn_M_phi_minus", "log_w": "L1_ffn_log_weights", "gumbel": "L1_ffn_gumbel",
}


def program(nc, io, out):
    io = dict(io)
    io["x"] = io["x"].rearrange("b h w c -> b (h w) c")
    m = Memory()
    with ExitStack() as ctx:
        sb = lambda n, s, d=fp32: ctx.enter_context(nc.sbuf_tensor(n, s, d))
        sem = lambda n: ctx.enter_context(nc.semaphore(n))
        m.gate_dram = nc.dram_tensor("gate_scratch", [NB, P, DT2, T], fp32, kind="Internal").ap()
        m.t_dram = nc.dram_tensor("token_scratch", [NB, T, C], fp32, kind="Internal").ap()
        m.t2_dram = nc.dram_tensor("attended_scratch", [NB, T, C], fp32, kind="Internal").ap()
        m.ident = sb("ident", [P, P])
        m.causal = sb("causal", [P, P])
        m.w_attn = sb("w_attn", [P, 3, C])
        m.b_qkv = sb("b_qkv", [P, 3])
        m.b_v = sb("b_v", [P, C])
        m.eps = sb("eps", [P, 2])
        m.idle = sb("idle", [P, NB])
        with ExitStack() as layer0:
            sb0 = lambda n, s, d=fp32: layer0.enter_context(nc.sbuf_tensor(n, s, d))
            m.group = sb0("group", [P, P])
            m.mean256 = sb0("mean256", [P, P])
            m.select = sb0("select", [P, 2 * NS, P], bf16)
            m.minus = sb0("minus", [P, 2, NS])
            m.part_mask = sb0("part_mask", [P, 2])
            m.w_conv = sb0("w_conv", [P, DT2, 9, P])
            m.w_z = sb0("w_z", [P, DT2, P])
            m.w_o = sb0("w_o", [P, DT2, P])
            m.xproj = sb0("xproj", [P, NK * DT2, P])
            m.w_dt = sb0("w_dt", [NR, NK * DT2, P])
            m.conv_b = sb0("conv_b", [P, DT2])
            m.dt_b = sb0("dt_b", [P, NK * DT2])
            m.a_neg = sb0("a_neg", [P, NK * DT2, NS])
            m.d_skip = sb0("d_skip", [P, 12])
            m.ln_w = sb0("ln_w", [P, DT2])
            m.ln_b = sb0("ln_b", [P, DT2])
            constants(nc, m, io)
            m.s1 = sb0("s1", [P, DT2, T])
            m.s2 = sb0("s2", [P, DT2, T])
            names = ["x_ch", "x_t", "gn", "gn_mm", "gn_sqrt", "normed", "gated", "conv_mm", "gate_mm",
                     "padded", "stats"]
            m.sem_a = {n: layer0.enter_context(nc.semaphore("a_" + n)) for n in names}
            m.sem_a["x_in"] = [layer0.enter_context(nc.semaphore(f"a_x_in{i}")) for i in range(4)]
            m.sem_a["gate_out"] = [layer0.enter_context(nc.semaphore(f"a_gate_out{i}")) for i in range(2)]
            m.sem_b = scan_semaphores(nc, layer0)
            m.sem_c = out_semaphores(nc, layer0)
            start_counts(nc, [*m.sem_a.values(), *m.sem_b.values(), *m.sem_c.values()])
            with nc.Fori(0, NB) as b:
                convolution(nc, m, io, b)
                with nc.sbuf_tensor("y", [P, DT2, T], fp32) as y:
                    m.y = y
                    scans(nc, m, b)
                    norm_and_project(nc, m, io, b)
        attention(nc, m, m.t2_dram)
        spectral(nc, m, io, out)


def kernel(**inputs):
    import concourse.bacc as bacc
    from concourse.bass_utils import run_bass_kernel_spmd

    nc = bacc.Bacc("TRN2", target_bir_lowering=False, num_devices=1)
    arrays, io = {}, {}
    for name, key in INPUTS.items():
        a = np.ascontiguousarray(inputs[key])
        arrays[f"in_{name}"] = a
        io[name] = nc.dram_tensor(f"in_{name}", a.shape, mybir.dt.from_np(a.dtype), kind="ExternalInput").ap()
    out = nc.dram_tensor("out", [NB, T, C], fp32, kind="ExternalOutput").ap()
    program(nc, io, out)
    r = run_bass_kernel_spmd(nc, [arrays], core_ids=[0])
    return r.results[0]["out"].reshape(NB, H, W, C)
```
